# Optimizing a Trainium2 kernel written in Bass

```python
import numpy as np
import jax
import jax.numpy as jnp

def _softmax(x, axis=-1):
    return jax.nn.softmax(x, axis=axis)

def _gelu(x):
    return jax.nn.gelu(x, approximate=True)

def _silu(x):
    return jax.nn.silu(x)

def _sigmoid(x):
    return jax.nn.sigmoid(x)

def _layernorm(x, axis=-1, eps=1e-05):
    m = jnp.mean(x, axis=axis, keepdims=True)
    v = jnp.var(x, axis=axis, keepdims=True)
    return (x - m) / jnp.sqrt(v + eps)

def _scatter_add(tgt, idx, src, axis=0):
    return tgt.at[idx].add(src)

def _segment_sum(src, seg, n):
    return jax.ops.segment_sum(src, seg, n)
kernel_name = 'mk_cond_resid_d1_seqx_r4_7a6903'

def setup_inputs(seed: int=0):
    np.random.seed(seed)
    _w = jnp.asarray

    def _rec_inputs():
        import jax
        import jax.numpy as jnp
        _rk = jax.random.key(seed)
        x = -0.000125 + 0.9999 * jax.random.normal(jax.random.fold_in(_rk, 1), (128, 64, 1024), jnp.float32)
        _lenS = 64 - jax.random.randint(jax.random.fold_in(_rk, 7), (128,), 0, max(1, 64 // 4) + 1, jnp.int32)
        _lenS2 = 64 - jax.random.randint(jax.random.fold_in(_rk, 8), (128,), 0, max(1, 64 // 4) + 1, jnp.int32)
        cond_128 = 0.0061147 + 1.02565 * jax.random.normal(jax.random.fold_in(_rk, 11), (128, 128), jnp.float32)
        return (x, cond_128)
    x, cond_128 = _rec_inputs()

    def _L0_cond_setup():
        import jax, jax.numpy as jnp
        import numpy as np
        K = 8
        T = 1.0
        D_EMBD = 128
        IN_C = 64
        OUT_C = 64
        BS = 32
        H = 1024
        HID = 128
        key = jax.random.key(seed)
        ks = jax.random.split(key, 10)
        s = lambda fan_in: 1.0 / np.sqrt(fan_in)
        return {'x': jax.random.normal(ks[0], (BS, IN_C, H), dtype=jnp.float32), 'embedding': jax.random.normal(ks[1], (BS, D_EMBD), dtype=jnp.float32), 'W0': jax.random.normal(ks[2], (D_EMBD, HID), dtype=jnp.float32) * s(D_EMBD), 'b0': jnp.zeros((HID,), dtype=jnp.float32), 'W1': jax.random.normal(ks[3], (HID, HID), dtype=jnp.float32) * s(HID), 'b1': jnp.zeros((HID,), dtype=jnp.float32), 'W2': jax.random.normal(ks[4], (HID, K), dtype=jnp.float32) * s(HID), 'b2': jnp.zeros((K,), dtype=jnp.float32), 'weight': jax.random.normal(ks[5], (K, OUT_C, IN_C, 1), dtype=jnp.float32) * s(IN_C), 'bias_k': jax.random.normal(ks[6], (K, OUT_C), dtype=jnp.float32) * 0.1}
    _L0_cond_all = _L0_cond_setup()
    _L0_cond_in = {k: v for k, v in _L0_cond_all.items() if k in ('W0', 'b0', 'W1', 'b1', 'W2', 'b2', 'weight', 'bias_k')}
    del _L0_cond_all
    return {'x': x, 'cond_128': cond_128, 'L0_cond_W0': _L0_cond_in['W0'], 'L0_cond_b0': _L0_cond_in['b0'], 'L0_cond_W1': _L0_cond_in['W1'], 'L0_cond_b1': _L0_cond_in['b1'], 'L0_cond_W2': _L0_cond_in['W2'], 'L0_cond_b2': _L0_cond_in['b2'], 'L0_cond_weight': _L0_cond_in['weight'], 'L0_cond_bias_k': _L0_cond_in['bias_k']}

def reference(x, cond_128, L0_cond_W0, L0_cond_b0, L0_cond_W1, L0_cond_b1, L0_cond_W2, L0_cond_b2, L0_cond_weight, L0_cond_bias_k):
    import jax
    import jax.numpy as jnp

    def _L0_cond_ref(x, embedding, W0, b0, W1, b1, W2, b2, weight, bias_k):
        import jax, jax.numpy as jnp
        import numpy as np
        K = 8
        T = 1.0
        D_EMBD = 128
        IN_C = 64
        OUT_C = 64
        BS = 32
        H = 1024
        HID = 128
        h = jax.nn.gelu(embedding @ W0 + b0, approximate=False)
        h = jax.nn.gelu(h @ W1 + b1, approximate=False)
        att = jax.nn.softmax((h @ W2 + b2) / T, axis=-1)
        agg_w = jnp.einsum('bk,koi->boi', att, weight[..., 0])
        agg_b = att @ bias_k
        out = jnp.einsum('boi,bih->boh', agg_w, x) + agg_b[:, :, None]
        return out
    x = x + _L0_cond_ref(x, cond_128, L0_cond_W0, L0_cond_b0, L0_cond_W1, L0_cond_b1, L0_cond_W2, L0_cond_b2, L0_cond_weight, L0_cond_bias_k)
    return x

_drawn_inputs = setup_inputs


def setup_inputs(seed=0):
    import zlib

    import numpy as np

    out = dict(_drawn_inputs(seed))
    spreads = {'L0_cond_b0': (0.0, 0.641), 'L0_cond_b1': (0.0, 0.357), 'L0_cond_b2': (0.0, 0.344)}
    factors = {}
    for name, (base, spread) in spreads.items():
        noise = np.random.default_rng([zlib.crc32(name.encode()), seed]).standard_normal(out[name].shape)
        drawn = base * np.exp(spread * noise) if base else spread * noise
        out[name] = jnp.asarray(drawn.astype(out[name].dtype))
    for name, factor in factors.items():
        out[name] = (out[name] * factor).astype(out[name].dtype)
    return out
```

```python
import concourse.bass as bass
from concourse import mybir
from contextlib import ExitStack


def cond_resid_kernel(nc, x, cond, w0, b0, w1, b1, w2, b2, weight, bias_k, out):
    fp32 = mybir.dt.float32
    ALU = mybir.AluOpType
    ACT = mybir.ActivationFunctionType
    AX = mybir.AxisListType

    B, C, H = x.shape
    K = weight.shape[0]
    P = 2 * C
    PAIRS = B // 2
    BANK = 512
    NB = 8
    HB = H // BANK
    PPT = 2
    TW = PPT * H
    TILES = PAIRS // PPT
    SEMS = 4
    SLOTS = 20
    BODIES = TILES // SEMS
    RING_BODIES = SLOTS // SEMS
    PPB = SEMS * PPT
    ACC = NB // HB
    OPB = BANK // PAIRS
    GROUPS = C // OPB
    ODD = 32
    KR = ODD + K
    WSLOTS = C * P // TW
    assert GROUPS == NB and ACC * HB == NB and SLOTS % SEMS == 0 and WSLOTS == SEMS
    assert B == P == cond.shape[1] == w0.shape[1] == w1.shape[1]

    x_tiles = x.rearrange("(t c s) i h -> t (s i) c h", c=PPT, s=2)
    out_tiles = out.rearrange("(t c s) i h -> t (s i) c h", c=PPT, s=2)

    ctx = ExitStack()
    with ctx:
        def sb(name, shape):
            return ctx.enter_context(nc.sbuf_tensor(name, shape, fp32))

        def sem(name):
            return ctx.enter_context(nc.semaphore(name))

        ring = sb("ring", [P, SLOTS * TW])
        wsets = ring[0:KR, (SLOTS - WSLOTS) * TW:SLOTS * TW].rearrange("k (o m) -> k o m", m=P)
        mixed = sb("mixed", [P, C, PAIRS])
        blocks = sb("blocks", [P, ACC, P])
        cond_sb = sb("cond_sb", [B, P])
        w0_sb = sb("w0_sb", [P, P])
        w1_sb = sb("w1_sb", [P, P])
        w2_sb = sb("w2_sb", [P, K])
        b0_sb = sb("b0_sb", [P, 1])
        b1_sb = sb("b1_sb", [P, 1])
        b2_sb = sb("b2_sb", [1, K])
        ones = sb("ones", [1, B])
        by_parity = sb("by_parity", [B, 2, PAIRS])
        fold = sb("fold", [B, PAIRS])
        cond_t = sb("cond_t", [P, B])
        h1_t = sb("h1_t", [P, B])
        h2_t = sb("h2_t", [P, B])
        neg_max = sb("neg_max", [B, 1])
        exps = sb("exps", [B, K])
        exp_sum = sb("exp_sum", [B, 1])
        inv_sum = sb("inv_sum", [B, 1])
        att_wide = sb("att_wide", [B, KR])
        att_pairs = sb("att_pairs", [KR, PAIRS])
        bias_sets = sb("bias_sets", [KR, P])
        bias_mixed = sb("bias_mixed", [P, PAIRS])

        psum = ctx.enter_context(nc.psum_tensor("psum", [P, NB * BANK], fp32))

        def bank(g, n):
            return psum[:, g * BANK:g * BANK + n]

        cond_ps, h1_ps, h2_ps = bank(7, B), bank(6, B), bank(5, B)
        logits_ps, att_ps, bias_ps = bank(4, K), psum[0:KR, 3 * BANK:3 * BANK + PAIRS], bank(7, PAIRS)

        cond_in, w0_in, w1_in, w2_in = sem("cond_in"), sem("w0_in"), sem("w1_in"), sem("w2_in")
        wsets_in, bias_sets_in = sem("wsets_in"), sem("bias_sets_in")
        x_in = [sem(f"x_in{k}") for k in range(SEMS)]
        stored = [sem(f"stored{k}") for k in range(SEMS)]
        perm_zeroed, perm_ready, fold_ready = sem("perm_zeroed"), sem("perm_ready"), sem("fold_ready")
        wsets_zeroed, blocks_zeroed = sem("wsets_zeroed"), sem("blocks_zeroed")
        small_zeroed = sem("small_zeroed")
        cond_turned, cond_copied = sem("cond_turned"), sem("cond_copied")
        h1_summed, h1_ready, h2_summed, h2_ready = sem("h1_summed"), sem("h1_ready"), sem("h2_summed"), sem("h2_ready")
        logits_ready, max_ready, exps_ready, inv_ready = (sem("logits_ready"), sem("max_ready"), sem("exps_ready"),
                                                          sem("inv_ready"))
        att_ready, att_folded, att_copied = sem("att_ready"), sem("att_folded"), sem("att_copied")
        bias_summed, bias_ready = sem("bias_summed"), sem("bias_ready")
        bank_mixed = sem("bank_mixed")
        copied_even, copied_odd = sem("copied_even"), sem("copied_odd")
        staged = sem("staged")
        multiplied = sem("multiplied")
        finished = sem("finished")

        block = ctx.enter_context(nc.Block())

        def slot_columns(first, t):
            return bass.ds((first + t) * TW, TW)

        @block.sync
        def _(sp):
            def load(tile, slot, k):
                sp.dma_start(ring[:, slot_columns(slot, 0)].rearrange("p (c h) -> p c h", c=PPT),
                             x_tiles[bass.ds(tile, 1)].rearrange("t p c h -> (t p) c h")).then_inc(x_in[k], 16)

            for k in range(SEMS):
                load(k, k, k)
            with sp.Fori(1, RING_BODIES - 1) as j:
                for k in range(SEMS):
                    sp.wait_ge(x_in[k], 16 * j)
                    load(SEMS * j + k, SEMS * j + k, k)
            sp.wait_ge(bank_mixed, GROUPS)
            for k in range(SEMS):
                sp.wait_ge(x_in[k], 16 * (RING_BODIES - 1))
                load(SLOTS - SEMS + k, SLOTS - SEMS + k, k)
            with sp.Fori(RING_BODIES, BODIES) as j:
                for k in range(SEMS):
                    sp.wait_ge(x_in[k], 16 * j)
                    sp.wait_ge(stored[k], 16 * (j - (RING_BODIES - 1)))
                    load(SEMS * j + k, SEMS * (j - RING_BODIES) + k, k)

        @block.gpsimd
        def _(pool):
            nc.gpsimd.memset(by_parity[:], 0.0).then_inc(perm_zeroed, 1)
            nc.gpsimd.memset(fold[:], 0.0).then_inc(perm_zeroed, 1)
            pool.wait_ge(perm_zeroed, 1)
            nc.gpsimd.affine_select(out=by_parity[:], in_=by_parity[:], compare_op=ALU.not_equal, fill=1.0, base=0,
                                    pattern=[[-1, 2], [-2, PAIRS]], channel_multiplier=1).then_inc(perm_ready, 1)
            pool.wait_ge(perm_zeroed, 2)
            nc.gpsimd.affine_select(out=fold[:], in_=fold[:], compare_op=ALU.not_equal, fill=1.0, base=0,
                                    pattern=[[-1, PAIRS]], channel_multiplier=1).then_inc(fold_ready, 1)
            pool.wait_ge(fold_ready, 1)
            nc.gpsimd.affine_select(out=fold[:], in_=fold[:], compare_op=ALU.not_equal, fill=1.0, base=-PAIRS,
                                    pattern=[[-1, PAIRS]], channel_multiplier=1).then_inc(fold_ready, 1)
            nc.gpsimd.memset(wsets[:, C // 2:C, :], 0.0).then_inc(wsets_zeroed, 1)

        @block.scalar
        def _(act):
            act.dma_start(cond_sb[:], cond).then_inc(cond_in, 16)
            act.dma_start(w0_sb[:], w0).then_inc(w0_in, 16)
            act.dma_start(b0_sb[:], b0.rearrange("(p a) -> p a", a=1)).then_inc(w0_in, 16)
            act.dma_start(w1_sb[:], w1).then_inc(w1_in, 16)
            act.dma_start(b1_sb[:], b1.rearrange("(p a) -> p a", a=1)).then_inc(w1_in, 16)
            act.dma_start(w2_sb[:], w2).then_inc(w2_in, 16)
            act.dma_start(b2_sb[:], b2.rearrange("(a k) -> a k", a=1)).then_inc(w2_in, 16)
            act.wait_ge(small_zeroed, 1)
            act.wait_ge(wsets_zeroed, 2)
            for s, row in enumerate((0, ODD)):
                act.dma_start(wsets[row:row + K, :, s * C:(s + 1) * C],
                              weight.rearrange("k o i a -> k o (i a)")).then_inc(wsets_in, 16)
                act.dma_start(bias_sets[row:row + K, s * C:(s + 1) * C], bias_k).then_inc(bias_sets_in, 16)

            act.wait_ge(w0_in, 32)
            act.wait_ge(h1_summed, 1)
            nc.scalar.activation(h1_t[:], h1_ps, ACT.Gelu, bias=b0_sb[:]).then_inc(h1_ready, 1)
            act.wait_ge(w1_in, 32)
            act.wait_ge(h2_summed, 1)
            nc.scalar.activation(h2_t[:], h2_ps, ACT.Gelu, bias=b1_sb[:]).then_inc(h2_ready, 1)
            act.wait_ge(max_ready, 1)
            nc.scalar.activation(exps[:], logits_ps, ACT.Exp, bias=neg_max[:],
                                 accum_out=exp_sum[:]).then_inc(exps_ready, 1)
            for g in range(1, GROUPS, 2):
                act.wait_ge(bank_mixed, g + 1)
                nc.scalar.copy(mixed[:, g * OPB:(g + 1) * OPB, :],
                               bank(g, BANK).rearrange("p (o n) -> p o n", o=OPB)).then_inc(copied_odd, 1)

            def stage(pair, a):
                for s in range(2):
                    rows = slice(s * C, (s + 1) * C)
                    last = nc.scalar.copy(blocks[rows, a, s * C:(s + 1) * C],
                                          mixed[rows, :, bass.ds(pair, 1)].rearrange("p o n -> p (o n)"))
                last.then_inc(staged, 1)

            def store(tile, slot, k):
                act.dma_start(out_tiles[bass.ds(tile, 1)].rearrange("t p c h -> (t p) c h"),
                              ring[:, slot_columns(slot, 0)].rearrange("p (c h) -> p c h", c=PPT)
                              ).then_inc(stored[k], 16)

            act.wait_ge(copied_even, GROUPS // 2)
            act.wait_ge(copied_odd, GROUPS // 2)
            act.wait_ge(blocks_zeroed, 1)
            for a in range(ACC):
                stage(a, a)

            def body(j, slot, first, last):
                for k in range(SEMS):
                    for c in range(PPT):
                        n = k * PPT + c
                        if not (last and n + ACC >= PPB):
                            act.wait_ge(multiplied, PPB * j + n + 1)
                            stage(PPB * j + n + ACC, n % ACC)
                    act.wait_ge(finished, PPB * j + (k + 1) * PPT)
                    if not first:
                        act.wait_ge(stored[k], 16 * j)
                    store(SEMS * j + k, slot + k, k)

            body(0, 0, True, False)
            with act.Fori(1, RING_BODIES) as j:
                body(j, SEMS * j, False, False)
            with act.Fori(RING_BODIES, BODIES - 1) as j:
                body(j, SEMS * (j - RING_BODIES), False, False)
            body(BODIES - 1, SEMS * (BODIES - 1 - RING_BODIES), False, True)
            for k in range(SEMS):
                act.wait_ge(stored[k], 16 * BODIES)

        @block.vector
        def _(dve):
            nc.vector.memset(wsets[:, 0:C // 2, :], 0.0).then_inc(wsets_zeroed, 1)
            nc.vector.memset(bias_sets[:], 0.0).then_inc(small_zeroed, 1)
            nc.vector.memset(ones[:], 1.0).then_inc(small_zeroed, 1)
            nc.vector.memset(att_wide[:], 0.0).then_inc(small_zeroed, 1)
            dve.wait_ge(cond_turned, 1)
            nc.vector.tensor_copy(cond_t[:], cond_ps).then_inc(cond_copied, 1)
            nc.vector.memset(blocks[:], 0.0).then_inc(blocks_zeroed, 1)
            dve.wait_ge(logits_ready, 1)
            nc.vector.tensor_reduce(out=neg_max[:], in_=logits_ps, axis=AX.X, op=ALU.max,
                                    negate=True).then_inc(max_ready, 1)
            dve.wait_ge(exps_ready, 1)
            nc.vector.reciprocal(inv_sum[:], exp_sum[:]).then_inc(inv_ready, 1)
            dve.wait_ge(inv_ready, 1)
            dve.wait_ge(small_zeroed, 3)
            nc.vector.tensor_scalar(att_wide[0:PAIRS, 0:K], exps[0:PAIRS, :], inv_sum[0:PAIRS, :], None, ALU.mult)
            nc.vector.tensor_scalar(att_wide[PAIRS:B, ODD:KR], exps[PAIRS:B, :], inv_sum[PAIRS:B, :], None,
                                    ALU.mult).then_inc(att_ready, 1)
            dve.wait_ge(att_folded, 1)
            nc.vector.tensor_copy(att_pairs[:], att_ps).then_inc(att_copied, 1)
            dve.wait_ge(bias_summed, 1)
            nc.vector.tensor_copy(bias_mixed[:], bias_ps).then_inc(bias_ready, 1)
            for g in range(0, GROUPS, 2):
                dve.wait_ge(bank_mixed, g + 1)
                nc.vector.tensor_copy(mixed[:, g * OPB:(g + 1) * OPB, :],
                                      bank(g, BANK).rearrange("p (o n) -> p o n", o=OPB)).then_inc(copied_even, 1)

            def body(j, first_column):
                for n in range(PPB):
                    dve.wait_ge(multiplied, PPB * j + n + 1)
                    columns = ring[:, bass.ds(first_column + n * H, H)]
                    a = n % ACC
                    nc.vector.scalar_tensor_tensor(
                        out=columns, in0=psum[:, a * H:(a + 1) * H], scalar=bias_mixed[:, bass.ds(PPB * j + n, 1)],
                        in1=columns, op0=ALU.add, op1=ALU.add).then_inc(finished, 1)

            dve.wait_ge(bias_ready, 1)
            with dve.Fori(0, RING_BODIES) as j:
                body(j, j * (PPB * H))
            with dve.Fori(RING_BODIES, BODIES) as j:
                body(j, (j - RING_BODIES) * (PPB * H))

        @block.tensor
        def _(pe):
            pe.wait_ge(cond_in, 16)
            pe.wait_ge(perm_ready, 1)
            nc.tensor.matmul(cond_ps, cond_sb[:], by_parity[:].rearrange("b s n -> b (s n)"),
                             start=True, stop=True).then_inc(cond_turned, 1)
            pe.wait_ge(w0_in, 32)
            pe.wait_ge(cond_copied, 1)
            nc.tensor.matmul(h1_ps, w0_sb[:], cond_t[:], start=True, stop=True).then_inc(h1_summed, 1)
            pe.wait_ge(w1_in, 32)
            pe.wait_ge(h1_ready, 1)
            nc.tensor.matmul(h2_ps, w1_sb[:], h1_t[:], start=True, stop=True).then_inc(h2_summed, 1)
            pe.wait_ge(w2_in, 32)
            pe.wait_ge(small_zeroed, 2)
            nc.tensor.matmul(logits_ps, ones[:], b2_sb[:], start=True, stop=False)
            pe.wait_ge(h2_ready, 1)
            nc.tensor.matmul(logits_ps, h2_t[:], w2_sb[:], start=False, stop=True).then_inc(logits_ready, 1)
            pe.wait_ge(fold_ready, 2)
            pe.wait_ge(att_ready, 1)
            nc.tensor.matmul(att_ps, att_wide[:], fold[:], start=True, stop=True).then_inc(att_folded, 1)
            pe.wait_ge(att_copied, 1)
            pe.wait_ge(bias_sets_in, 32)
            nc.tensor.matmul(bias_ps, bias_sets[:], att_pairs[:], start=True, stop=True).then_inc(bias_summed, 1)
            pe.wait_ge(wsets_in, 32)
            for g in range(GROUPS):
                if g == NB - 1:
                    pe.wait_ge(bias_ready, 1)
                for o in range(g * OPB, (g + 1) * OPB):
                    last = nc.tensor.matmul(psum[:, o * PAIRS:(o + 1) * PAIRS], wsets[:, o, :], att_pairs[:],
                                            start=True, stop=True)
                last.then_inc(bank_mixed, 1)

            def body(j, first_column, first):
                for k in range(SEMS):
                    pe.wait_ge(x_in[k], 16 * j + 16)
                    for c in range(PPT):
                        n = k * PPT + c
                        a = n % ACC
                        pe.wait_ge(staged, PPB * j + n + 1)
                        if not (first and n < ACC):
                            pe.wait_ge(finished, PPB * j + n - ACC + 1)
                        for b in range(HB):
                            last = nc.tensor.matmul(psum[:, (a * HB + b) * BANK:(a * HB + b + 1) * BANK],
                                                    blocks[:, a, :],
                                                    ring[:, bass.ds(first_column + n * H + b * BANK, BANK)],
                                                    start=True, stop=True)
                        last.then_inc(multiplied, 1)

            body(0, 0, True)
            with pe.Fori(1, RING_BODIES) as j:
                body(j, j * (PPB * H), False)
            with pe.Fori(RING_BODIES, BODIES) as j:
                body(j, (j - RING_BODIES) * (PPB * H), False)


_INS = ["x", "cond_128", "L0_cond_W0", "L0_cond_b0", "L0_cond_W1", "L0_cond_b1", "L0_cond_W2", "L0_cond_b2",
        "L0_cond_weight", "L0_cond_bias_k"]


def kernel(**inputs):
    import numpy as _np
    import concourse.bacc as _bacc
    from concourse import mybir as _mybir
    from concourse.bass_utils import run_bass_kernel_spmd as _run

    nc = _bacc.Bacc("TRN2", target_bir_lowering=False, num_devices=1)
    arrays, args = {}, []
    for name in _INS:
        a = _np.ascontiguousarray(inputs[name])
        arrays[f"in_{name}_dram"] = a
        args.append(nc.dram_tensor(f"in_{name}_dram", a.shape, _mybir.dt.from_np(a.dtype), kind="ExternalInput").ap())
    x = arrays["in_x_dram"]
    args.append(nc.dram_tensor("out_dram", x.shape, _mybir.dt.from_np(x.dtype), kind="ExternalOutput").ap())
    cond_resid_kernel(nc, *args)
    r = _run(nc, [arrays], core_ids=[0])
    return r.results[0]["out_dram"]
```

```python
import concourse.bass as bass
from concourse import mybir
from contextlib import ExitStack


def cond_resid_kernel(nc, x, cond, w0, b0, w1, b1, w2, b2, weight, bias_k, out):
    fp32 = mybir.dt.float32
    ALU = mybir.AluOpType
    ACT = mybir.ActivationFunctionType
    AX = mybir.AxisListType

    B, C, H = x.shape
    K = weight.shape[0]
    P = 2 * C
    PAIRS = B // 2
    BANK = 512
    NB = 8
    HB = H // BANK
    PPT = 2
    TW = PPT * H
    TILES = PAIRS // PPT
    SEMS = 4
    SLOTS = 20
    BODIES = TILES // SEMS
    RING_BODIES = SLOTS // SEMS
    PPB = SEMS * PPT
    ACC = NB // HB
    OPB = BANK // B
    GROUPS = C // 2 // OPB
    assert GROUPS == NB and ACC * HB == NB and SLOTS % SEMS == 0 and TILES % SEMS == 0
    assert B == P == cond.shape[1] == w0.shape[1] == w1.shape[1]

    x_tiles = x.rearrange("(t c s) i h -> t (s i) c h", c=PPT, s=2)
    out_tiles = out.rearrange("(t c s) i h -> t (s i) c h", c=PPT, s=2)

    ctx = ExitStack()
    with ctx:
        def sb(name, shape):
            return ctx.enter_context(nc.sbuf_tensor(name, shape, fp32))

        def sem(name):
            return ctx.enter_context(nc.semaphore(name))

        ring = sb("ring", [P, SLOTS * TW])
        wsets = sb("wsets", [K, C // 2, P])
        mixed = sb("mixed", [P, C // 2, 2, PAIRS])
        blocks = sb("blocks", [P, ACC, P])
        cond_sb = sb("cond_sb", [B, P])
        w0_sb = sb("w0_sb", [P, P])
        w1_sb = sb("w1_sb", [P, P])
        w2_sb = sb("w2_sb", [P, K])
        b0_sb = sb("b0_sb", [1, P])
        b1_sb = sb("b1_sb", [1, P])
        b2_sb = sb("b2_sb", [1, K])
        ones = sb("ones", [1, B])
        identity = sb("identity", [P, P])
        cond_t = sb("cond_t", [P, B])
        h1_t = sb("h1_t", [P, B])
        h2_t = sb("h2_t", [P, B])
        neg_max = sb("neg_max", [B, 1])
        exps = sb("exps", [B, K])
        exp_sum = sb("exp_sum", [B, 1])
        inv_sum = sb("inv_sum", [B, 1])
        att = sb("att", [B, K])
        att_t = sb("att_t", [K, 2, PAIRS])
        bias_sets = sb("bias_sets", [K, C])
        bias_mixed = sb("bias_mixed", [P, PAIRS])

        psum = ctx.enter_context(nc.psum_tensor("psum", [P, NB * BANK], fp32))

        def bank(g, n):
            return psum[:, g * BANK:g * BANK + n]

        cond_ps, h1_ps, h2_ps = bank(7, B), bank(6, B), bank(5, B)
        logits_ps, att_ps, bias_ps = bank(4, K), psum[0:K, 3 * BANK:3 * BANK + B], psum[0:C, 7 * BANK:7 * BANK + B]

        cond_in, w0_in, w1_in, w2_in = sem("cond_in"), sem("w0_in"), sem("w1_in"), sem("w2_in")
        wsets_in, bias_sets_in = sem("wsets_in"), sem("bias_sets_in")
        x_in = [sem(f"x_in{k}") for k in range(SEMS)]
        stored = [sem(f"stored{k}") for k in range(SEMS)]
        identity_zeroed, identity_ready = sem("identity_zeroed"), sem("identity_ready")
        ones_ready, blocks_zeroed = sem("ones_ready"), sem("blocks_zeroed")
        cond_turned, cond_copied = sem("cond_turned"), sem("cond_copied")
        h1_summed, h1_ready, h2_summed, h2_ready = sem("h1_summed"), sem("h1_ready"), sem("h2_summed"), sem("h2_ready")
        logits_ready, max_ready, exps_ready, inv_ready = (sem("logits_ready"), sem("max_ready"), sem("exps_ready"),
                                                          sem("inv_ready"))
        att_ready, att_turned, att_copied = sem("att_ready"), sem("att_turned"), sem("att_copied")
        bias_summed, bias_ready = sem("bias_summed"), sem("bias_ready")
        bank_mixed = sem("bank_mixed")
        copied_even, copied_odd = sem("copied_even"), sem("copied_odd")
        staged = sem("staged")
        multiplied = sem("multiplied")
        finished = sem("finished")

        block = ctx.enter_context(nc.Block())

        def slot_columns(slot):
            return bass.ds(slot * TW, TW)

        def mixed_quarters(g):
            for r in range(2):
                for s in range(2):
                    yield (mixed[s * C:(s + 1) * C, g * OPB:(g + 1) * OPB, r, :],
                           bank(g, BANK)[r * C:(r + 1) * C, :].rearrange("p (o s n) -> p o s n", s=2, n=PAIRS)
                           [:, :, s, :])

        @block.sync
        def _(sp):
            def load(tile, slot, k):
                sp.dma_start(ring[:, slot_columns(slot)].rearrange("p (c h) -> p c h", c=PPT),
                             x_tiles[bass.ds(tile, 1)].rearrange("t p c h -> (t p) c h")).then_inc(x_in[k], 16)

            for k in range(SEMS):
                load(k, k, k)
            with sp.Fori(1, RING_BODIES) as j:
                for k in range(SEMS):
                    sp.wait_ge(x_in[k], 16 * j)
                    load(SEMS * j + k, SEMS * j + k, k)
            with sp.Fori(RING_BODIES, BODIES) as j:
                for k in range(SEMS):
                    sp.wait_ge(x_in[k], 16 * j)
                    sp.wait_ge(stored[k], 16 * (j - (RING_BODIES - 1)))
                    load(SEMS * j + k, SEMS * (j - RING_BODIES) + k, k)

        @block.gpsimd
        def _(pool):
            nc.gpsimd.memset(identity[:], 0.0).then_inc(identity_zeroed, 1)
            pool.wait_ge(identity_zeroed, 1)
            nc.gpsimd.affine_select(out=identity[:], in_=identity[:], compare_op=ALU.not_equal, fill=1.0, base=0,
                                    pattern=[[-1, P]], channel_multiplier=1).then_inc(identity_ready, 1)
            nc.gpsimd.memset(blocks[:], 0.0).then_inc(blocks_zeroed, 1)

            def stage(pair, a):
                for s in range(2):
                    rows = slice(s * C, (s + 1) * C)
                    last = nc.gpsimd.tensor_copy(blocks[rows, a, s * C:(s + 1) * C],
                                                 mixed[rows, :, :, bass.ds(pair, 1)].rearrange("p o r n -> p (o r n)"))
                last.then_inc(staged, 1)

            pool.wait_ge(blocks_zeroed, 1)
            pool.wait_ge(copied_even, GROUPS // 2)
            pool.wait_ge(copied_odd, GROUPS // 2)
            for a in range(ACC):
                stage(a, a)
            with pool.Fori(0, PAIRS // ACC - 1) as j:
                for a in range(ACC):
                    pool.wait_ge(multiplied, ACC * j + a + 1)
                    stage(ACC * j + ACC + a, a)

        @block.scalar
        def _(act):
            act.dma_start(cond_sb[:], cond).then_inc(cond_in, 16)
            act.dma_start(w0_sb[:], w0).then_inc(w0_in, 16)
            act.dma_start(b0_sb[:], b0.rearrange("(a p) -> a p", a=1)).then_inc(w0_in, 16)
            act.dma_start(w1_sb[:], w1).then_inc(w1_in, 16)
            act.dma_start(b1_sb[:], b1.rearrange("(a p) -> a p", a=1)).then_inc(w1_in, 16)
            act.dma_start(w2_sb[:], w2).then_inc(w2_in, 16)
            act.dma_start(b2_sb[:], b2.rearrange("(a k) -> a k", a=1)).then_inc(w2_in, 16)
            act.dma_start(wsets[:].rearrange("k o m -> k (o m)"),
                          weight.rearrange("k o i a -> k (o i a)")).then_inc(wsets_in, 16)
            act.dma_start(bias_sets[:], bias_k).then_inc(bias_sets_in, 16)

            act.wait_ge(h1_summed, 1)
            nc.scalar.activation(h1_t[:], h1_ps, ACT.Gelu).then_inc(h1_ready, 1)
            act.wait_ge(h2_summed, 1)
            nc.scalar.activation(h2_t[:], h2_ps, ACT.Gelu).then_inc(h2_ready, 1)
            act.wait_ge(max_ready, 1)
            nc.scalar.activation(exps[:], logits_ps, ACT.Exp, bias=neg_max[:],
                                 accum_out=exp_sum[:]).then_inc(exps_ready, 1)
            for g in range(1, GROUPS, 2):
                act.wait_ge(bank_mixed, g + 1)
                for to, source in mixed_quarters(g):
                    last = nc.scalar.copy(to, source)
                last.then_inc(copied_odd, 1)

            def store(tile, slot, k):
                act.dma_start(out_tiles[bass.ds(tile, 1)].rearrange("t p c h -> (t p) c h"),
                              ring[:, slot_columns(slot)].rearrange("p (c h) -> p c h", c=PPT)
                              ).then_inc(stored[k], 16)

            def body(j, slot, first):
                for k in range(SEMS):
                    act.wait_ge(finished, PPB * j + (k + 1) * PPT)
                    if not first:
                        act.wait_ge(stored[k], 16 * j)
                    store(SEMS * j + k, slot + k, k)

            body(0, 0, True)
            with act.Fori(1, RING_BODIES) as j:
                body(j, SEMS * j, False)
            with act.Fori(RING_BODIES, BODIES) as j:
                body(j, SEMS * (j - RING_BODIES), False)
            for k in range(SEMS):
                act.wait_ge(stored[k], 16 * BODIES)

        @block.vector
        def _(dve):
            nc.vector.memset(ones[:], 1.0).then_inc(ones_ready, 1)
            dve.wait_ge(cond_turned, 1)
            nc.vector.tensor_copy(cond_t[:], cond_ps).then_inc(cond_copied, 1)
            dve.wait_ge(logits_ready, 1)
            nc.vector.tensor_reduce(out=neg_max[:], in_=logits_ps, axis=AX.X, op=ALU.max,
                                    negate=True).then_inc(max_ready, 1)
            dve.wait_ge(exps_ready, 1)
            nc.vector.reciprocal(inv_sum[:], exp_sum[:]).then_inc(inv_ready, 1)
            dve.wait_ge(inv_ready, 1)
            nc.vector.tensor_scalar(att[:], exps[:], inv_sum[:], None, ALU.mult).then_inc(att_ready, 1)
            dve.wait_ge(att_turned, 1)
            nc.vector.tensor_copy(att_t[:], att_ps.rearrange("k (n s) -> k s n", s=2)).then_inc(att_copied, 1)
            dve.wait_ge(bias_summed, 1)
            for s in range(2):
                last = nc.vector.tensor_copy(bias_mixed[s * C:(s + 1) * C, :], bias_ps[:, s * PAIRS:(s + 1) * PAIRS])
            last.then_inc(bias_ready, 1)
            for g in range(0, GROUPS, 2):
                dve.wait_ge(bank_mixed, g + 1)
                for to, source in mixed_quarters(g):
                    last = nc.vector.tensor_copy(to, source)
                last.then_inc(copied_even, 1)

            def body(j, first_column):
                for n in range(PPB):
                    dve.wait_ge(multiplied, PPB * j + n + 1)
                    columns = ring[:, bass.ds(first_column + n * H, H)]
                    a = n % ACC
                    nc.vector.scalar_tensor_tensor(
                        out=columns, in0=psum[:, a * H:(a + 1) * H], scalar=bias_mixed[:, bass.ds(PPB * j + n, 1)],
                        in1=columns, op0=ALU.add, op1=ALU.add).then_inc(finished, 1)

            dve.wait_ge(bias_ready, 1)
            with dve.Fori(0, RING_BODIES) as j:
                body(j, j * (PPB * H))
            with dve.Fori(RING_BODIES, BODIES) as j:
                body(j, (j - RING_BODIES) * (PPB * H))

        @block.tensor
        def _(pe):
            pe.wait_ge(cond_in, 16)
            pe.wait_ge(identity_ready, 1)
            nc.tensor.transpose(cond_ps, cond_sb[:], identity[:]).then_inc(cond_turned, 1)
            pe.wait_ge(w0_in, 32)
            pe.wait_ge(ones_ready, 1)
            nc.tensor.matmul(h1_ps, b0_sb[:], ones[:], start=True, stop=False)
            pe.wait_ge(cond_copied, 1)
            nc.tensor.matmul(h1_ps, w0_sb[:], cond_t[:], start=False, stop=True).then_inc(h1_summed, 1)
            pe.wait_ge(w1_in, 32)
            nc.tensor.matmul(h2_ps, b1_sb[:], ones[:], start=True, stop=False)
            pe.wait_ge(h1_ready, 1)
            nc.tensor.matmul(h2_ps, w1_sb[:], h1_t[:], start=False, stop=True).then_inc(h2_summed, 1)
            pe.wait_ge(w2_in, 32)
            nc.tensor.matmul(logits_ps, ones[:], b2_sb[:], start=True, stop=False)
            pe.wait_ge(h2_ready, 1)
            nc.tensor.matmul(logits_ps, h2_t[:], w2_sb[:], start=False, stop=True).then_inc(logits_ready, 1)
            pe.wait_ge(att_ready, 1)
            nc.tensor.transpose(att_ps, att[:], identity[:]).then_inc(att_turned, 1)
            columns = att_t[:].rearrange("k s n -> k (s n)")
            pe.wait_ge(att_copied, 1)
            pe.wait_ge(bias_sets_in, 16)
            nc.tensor.matmul(bias_ps, bias_sets[:], columns, start=True, stop=True).then_inc(bias_summed, 1)
            pe.wait_ge(wsets_in, 16)
            for g in range(GROUPS):
                if g == NB - 1:
                    pe.wait_ge(bias_ready, 1)
                for o in range(g * OPB, (g + 1) * OPB):
                    last = nc.tensor.matmul(psum[:, o * B:(o + 1) * B], wsets[:, o, :], columns,
                                            start=True, stop=True)
                last.then_inc(bank_mixed, 1)

            def body(j, first_column, first):
                for k in range(SEMS):
                    pe.wait_ge(x_in[k], 16 * j + 16)
                    for c in range(PPT):
                        n = k * PPT + c
                        a = n % ACC
                        pe.wait_ge(staged, PPB * j + n + 1)
                        if not (first and n < ACC):
                            pe.wait_ge(finished, PPB * j + n - ACC + 1)
                        for b in range(HB):
                            last = nc.tensor.matmul(psum[:, (a * HB + b) * BANK:(a * HB + b + 1) * BANK],
                                                    blocks[:, a, :],
                                                    ring[:, bass.ds(first_column + n * H + b * BANK, BANK)],
                                                    start=True, stop=True)
                        last.then_inc(multiplied, 1)

            body(0, 0, True)
            with pe.Fori(1, RING_BODIES) as j:
                body(j, j * (PPB * H), False)
            with pe.Fori(RING_BODIES, BODIES) as j:
                body(j, (j - RING_BODIES) * (PPB * H), False)


_INS = ["x", "cond_128", "L0_cond_W0", "L0_cond_b0", "L0_cond_W1", "L0_cond_b1", "L0_cond_W2", "L0_cond_b2",
        "L0_cond_weight", "L0_cond_bias_k"]


def kernel(**inputs):
    import numpy as _np
    import concourse.bacc as _bacc
    from concourse import mybir as _mybir
    from concourse.bass_utils import run_bass_kernel_spmd as _run

    nc = _bacc.Bacc("TRN2", target_bir_lowering=False, num_devices=1)
    arrays, args = {}, []
    for name in _INS:
        a = _np.ascontiguousarray(inputs[name])
        arrays[f"in_{name}_dram"] = a
        args.append(nc.dram_tensor(f"in_{name}_dram", a.shape, _mybir.dt.from_np(a.dtype), kind="ExternalInput").ap())
    x = arrays["in_x_dram"]
    args.append(nc.dram_tensor("out_dram", x.shape, _mybir.dt.from_np(x.dtype), kind="ExternalOutput").ap())
    cond_resid_kernel(nc, *args)
    r = _run(nc, [arrays], core_ids=[0])
    return r.results[0]["out_dram"]
```
